# Optimizing a Trainium2 kernel written in Bass

```python
import numpy as np
import jax
import jax.numpy as jnp

def _softmax(x, axis=-1):
    return jax.nn.softmax(x, axis=axis)

def _gelu(x):
    return jax.nn.gelu(x, approximate=True)

def _silu(x):
    return jax.nn.silu(x)

def _sigmoid(x):
    return jax.nn.sigmoid(x)

def _layernorm(x, axis=-1, eps=1e-05):
    m = jnp.mean(x, axis=axis, keepdims=True)
    v = jnp.var(x, axis=axis, keepdims=True)
    return (x - m) / jnp.sqrt(v + eps)

def _scatter_add(tgt, idx, src, axis=0):
    return tgt.at[idx].add(src)

def _segment_sum(src, seg, n):
    return jax.ops.segment_sum(src, seg, n)
kernel_name = 'mk_xattn_ffn_d1_seqx_r4_a539ad'

def setup_inputs(seed: int=0):
    np.random.seed(seed)
    _w = jnp.asarray

    def _rec_inputs():
        import jax
        import jax.numpy as jnp
        _rk = jax.random.key(seed)
        x = 0.0003765 + 1 * jax.random.normal(jax.random.fold_in(_rk, 1), (8, 256, 512), jnp.float32)
        _lenS = 256 - jax.random.randint(jax.random.fold_in(_rk, 7), (8,), 0, max(1, 256 // 4) + 1, jnp.int32)
        _lenS2 = 256 - jax.random.randint(jax.random.fold_in(_rk, 8), (8,), 0, max(1, 256 // 4) + 1, jnp.int32)
        _ctx_2048P = jax.random.normal(jax.random.fold_in(_rk, 11), (8, 16, 512), jnp.float32)
        _ctx_2048c = jax.random.dirichlet(jax.random.fold_in(_rk, 511), 0.3 * jnp.ones((16,), jnp.float32), (8, 256))
        _ctx_2048t = jnp.einsum('bsk,bkd->bsd', _ctx_2048c, _ctx_2048P)
        _ctx_2048t = _ctx_2048t * jax.lax.rsqrt(jnp.mean(jnp.square(_ctx_2048t)) + 1e-12) * 0.953939
        ctx_2048 = -0.000292821 + 1.00034 * (_ctx_2048t + 0.3 * jax.random.normal(jax.random.fold_in(_rk, 611), (8, 256, 512), jnp.float32))
        return (x, ctx_2048)
    x, ctx_2048 = _rec_inputs()

    def _L0_xattn_setup():
        import jax, jax.numpy as jnp
        import numpy as np
        key = jax.random.key(seed)
        k1, k2, k3, k4, k5 = jax.random.split(key, 5)
        B, D_MODEL, L = (2, 256, 512)
        HEAD_DIM = 8
        H = D_MODEL // HEAD_DIM
        return {'k': jax.random.normal(k1, (B, D_MODEL, L), dtype=jnp.float32), 'v': jax.random.normal(k2, (B, D_MODEL, L), dtype=jnp.float32), 'q': jax.random.normal(k3, (B, D_MODEL, L), dtype=jnp.float32), 'ssm_kernel': jax.random.normal(k4, (H, L), dtype=jnp.float32), 'D': jax.random.normal(k5, (H,), dtype=jnp.float32), 'head_dim': HEAD_DIM}
    _L0_xattn_all = _L0_xattn_setup()
    _L0_xattn_in = {k: v for k, v in _L0_xattn_all.items() if k in ('ssm_kernel', 'D')}
    del _L0_xattn_all

    def _L0_ffn_setup():
        import jax, jax.numpy as jnp
        import numpy as np
        HIDDEN = 512
        INTER = 2048
        BATCH, LOCAL_SEQ = (2, 1024)
        key = jax.random.key(seed)
        k1, k2, k3 = jax.random.split(key, 3)
        h_shard = jax.random.normal(k1, (BATCH, LOCAL_SEQ, HIDDEN), dtype=jnp.float32)
        w_gate_up = jax.random.normal(k2, (2 * INTER, HIDDEN), dtype=jnp.float32) * 0.02
        w_down = jax.random.normal(k3, (HIDDEN, INTER), dtype=jnp.float32) * 0.02
        return {'h_shard': h_shard, 'w_gate_up': w_gate_up, 'w_down': w_down}
    _L0_ffn_all = _L0_ffn_setup()
    _L0_ffn_in = {k: v for k, v in _L0_ffn_all.items() if k in ('w_gate_up', 'w_down')}
    del _L0_ffn_all
    return {'x': x, 'ctx_2048': ctx_2048, 'L0_xattn_ssm_kernel': _L0_xattn_in['ssm_kernel'], 'L0_xattn_D': _L0_xattn_in['D'], 'L0_ffn_w_gate_up': _L0_ffn_in['w_gate_up'], 'L0_ffn_w_down': _L0_ffn_in['w_down']}

def reference(x, ctx_2048, L0_xattn_ssm_kernel, L0_xattn_D, L0_ffn_w_gate_up, L0_ffn_w_down):
    import jax
    import jax.numpy as jnp

    def _L0_xattn_ref(k, v, q, ssm_kernel, D, head_dim):
        import jax, jax.numpy as jnp
        import numpy as np
        B, HD, L = k.shape
        H = HD // head_dim
        fft_size = 2 * L
        k_ = k.reshape(B, H, head_dim, L)
        v_ = v.reshape(B, H, head_dim, L)
        q_ = q.reshape(B, H, head_dim, L)
        kv = jnp.einsum('bhil,bhjl->bijhl', k_, v_)
        kv_f = jnp.fft.rfft(kv, n=fft_size)
        kernel_f = jnp.fft.rfft(ssm_kernel, n=fft_size)
        y = jnp.fft.irfft(kv_f * kernel_f, n=fft_size)[..., :L]
        out = y + kv * D[None, None, None, :, None]
        out = jnp.einsum('bijhl,bhil->bjhl', out, q_)
        out = jnp.transpose(out, (0, 2, 1, 3)).reshape(B, H * head_dim, L)
        return out.astype(k.dtype)

    def _L0_ffn_ref(h_shard, w_gate_up, w_down):
        import jax, jax.numpy as jnp
        import numpy as np
        HIDDEN = 512
        INTER = 2048
        BATCH, LOCAL_SEQ = (2, 1024)
        batch, local_seq, hidden = h_shard.shape
        gate_up = jnp.einsum('bsh,oh->bso', h_shard, w_gate_up)
        gate, up = jnp.split(gate_up, 2, axis=-1)
        h = jax.nn.silu(gate) * up
        out = jnp.einsum('bsi,hi->bsh', h, w_down)
        return out
    x = x + _L0_xattn_ref(ctx_2048, ctx_2048, _layernorm(x, axis=-1), L0_xattn_ssm_kernel, L0_xattn_D, 8)
    x = x + _L0_ffn_ref(_layernorm(x, axis=-1), L0_ffn_w_gate_up, L0_ffn_w_down)
    return x

_drawn_inputs = setup_inputs


def setup_inputs(seed=0):
    import zlib

    import numpy as np

    out = dict(_drawn_inputs(seed))
    spreads = {}
    factors = {'L0_ffn_w_gate_up': 8.0, 'L0_ffn_w_down': 8.0}
    for name, (base, spread) in spreads.items():
        noise = np.random.default_rng([zlib.crc32(name.encode()), seed]).standard_normal(out[name].shape)
        drawn = base * np.exp(spread * noise) if base else spread * noise
        out[name] = jnp.asarray(drawn.astype(out[name].dtype))
    for name, factor in factors.items():
        out[name] = (out[name] * factor).astype(out[name].dtype)
    return out
```

```python
from contextlib import ExitStack

import concourse.bass as bass
from concourse import mybir

P = 128
ALU = mybir.AluOpType
ACT = mybir.ActivationFunctionType
F32 = mybir.dt.float32
F32R = mybir.dt.float32r
AX_X = mybir.AxisListType.X
EPS = 1e-5


def xattn_ffn(nc, x, ctx, ssm_kernel, skip, w_gate_up, w_down, out):
    B, S, L = x.shape
    H = ssm_kernel.shape[0]
    HD = S // H
    INTER = w_down.shape[1]
    LB = L // P
    STEP_HEADS = 4
    STEP_ROWS = STEP_HEADS * HD
    STEPS = H // STEP_HEADS
    BLOCK_BATCHES = P // STEP_ROWS
    STEP_BLOCKS = B // BLOCK_BATCHES
    BLOCKS = STEPS * STEP_BLOCKS
    TILE_BLOCKS = 4
    TILES = BLOCKS // TILE_BLOCKS
    TILE = TILE_BLOCKS * P
    DIAG = HD // 2
    PAIRS = DIAG * HD + DIAG
    CW = HD + DIAG
    QW = 2 * HD
    YW = DIAG * 2 * HD + DIAG
    TERMS = HD
    JB = LB * B
    PAD = P - 1
    CHUNKS = 2
    GROUPS = INTER // (CHUNKS * P)
    W_UNITS = 3 * CHUNKS
    WNAT = 4
    GROUP_UNITS = TILES
    assert (LB, STEPS, STEP_BLOCKS, TILES, DIAG) == (4, 8, 2, 4, 4)
    PARTS = ((0, 0), (0, 1), (1, 0))

    KROW = PAD + L + 1
    kpad_dram = nc.dram_tensor("kpad", (H, KROW), F32)
    kpad = kpad_dram.ap()
    toeplitz = bass.AP(tensor=kpad_dram, offset=0, ap=[[KROW, H], [1, P], [1, L]])

    with ExitStack() as stack:
        def sb(name, shape, dt=F32, where=stack):
            return where.enter_context(nc.sbuf_tensor(name, shape, dt))

        def sem(name):
            return stack.enter_context(nc.semaphore(name))

        ident = sb("ident", [P, P])
        flip = sb("flip", [P, P])
        acc = sb("acc", [P, BLOCKS * L])
        hT = [sb("hT_hi", [P, TILES * LB * TILE], F32R), sb("hT_lo", [P, TILES * LB * TILE], F32R)]
        w_slot = [[sb("w0_hi", [P, W_UNITS * 512], F32R), sb("w0_lo", [P, W_UNITS * 512], F32R)]]
        wnat = sb("wnat", [P, WNAT, 512])
        stats = sb("stats", [P, 4, 6])
        meanvar = sb("meanvar", [P, 4, 2])
        vareps = sb("vareps", [P, 4])
        rstd = sb("rstd", [P, 4])
        minus_half = sb("minus_half", [P, 4])

        phase_a = ExitStack()
        with phase_a:
            cnat = sb("cnat", [P, 2, L], F32, phase_a)
            normed = sb("normed", [P, 2, L], F32, phase_a)
            cT = sb("cT", [P, JB * STEP_HEADS * CW], F32, phase_a)
            qT = [sb(f"qT{i}", [P, JB * STEP_HEADS * QW], F32, phase_a) for i in range(2)]
            kv = [sb(f"kv{i}", [P, JB * PAIRS], F32, phase_a) for i in range(2)]
            toep = [sb(f"toep{i}", [P, L], F32, phase_a) for i in range(2)]
            ysb = [sb(f"ysb{i}", [P, JB * YW], F32, phase_a) for i in range(2)]
            prod = sb("prod", [P, JB * TERMS * HD], F32, phase_a)
            oT = [sb(f"oT{i}", [P, JB * STEP_ROWS], F32, phase_a) for i in range(2)]
        kp = prod[0:H, 0:KROW]
        k_loaded = prod[0:H, KROW:KROW + L]
        dcol = prod[0:H, KROW + L:KROW + L + 1]
        w_slot.append([sb("w1_hi", [P, W_UNITS * 512], F32R), sb("w1_lo", [P, W_UNITS * 512], F32R)])
        a_part = [[sb(f"a{i}_{n}", [P, CHUNKS * TILE], F32R) for n in ("hi", "lo")] for i in range(2)]
        a_full = sb("a_full", [P, 2, TILE])

        ps = stack.enter_context(nc.psum_tensor("ps", [P, 8, 512], F32))

        waits_passed = sem("waits_passed")
        ident_ready = sem("ident_ready")
        consts_ready = sem("consts_ready")
        kp_loaded = sem("kp_loaded")
        kp_ready = sem("kp_ready")
        kpad_written = sem("kpad_written")
        cx_loaded = [sem(f"cx_loaded{i}") for i in range(2)]
        toep_loaded = [sem(f"toep_loaded{i}") for i in range(2)]
        stats_done = sem("stats_done")
        vareps_done = sem("vareps_done")
        aggr_done = sem("aggr_done")
        rstd_ready = sem("rstd_ready")
        q_normed = sem("q_normed")
        h_normed = sem("h_normed")
        c_transposed = sem("c_transposed")
        q_transposed = sem("q_transposed")
        o_transposed = sem("o_transposed")
        h_transposed = sem("h_transposed")
        c_evac = sem("c_evac")
        q_evac = sem("q_evac")
        kv_ready = sem("kv_ready")
        y_ready = sem("y_ready")
        y_evac = sem("y_evac")
        multiplied = sem("multiplied")
        reduced = sem("reduced")
        o_added = sem("o_added")
        h_hi = sem("h_hi")
        h_split = sem("h_split")
        wnat_loaded = [sem(f"wnat_loaded{i}") for i in range(WNAT)]
        w_transposed = sem("w_transposed")
        w_hi = sem("w_hi")
        w_split = sem("w_split")
        gate_up_ready = sem("gate_up_ready")
        silu_ready = sem("silu_ready")
        product_done = sem("product_done")
        a_hi = sem("a_hi")
        a_split = sem("a_split")
        d_ready = sem("d_ready")
        added = sem("added")
        stored = sem("stored")
        GU_FREE, A_FREE, D_FREE, H_FREE = 2, 2, 2, 2
        DOWN_FREE = 2 * TILE_BLOCKS

        block = stack.enter_context(nc.Block())

        def rows(dram, n, bb):
            return dram[bb * BLOCK_BATCHES:(bb + 1) * BLOCK_BATCHES, bass.ds(n * STEP_ROWS, STEP_ROWS), :]

        def acc_of(n, bb):
            return acc[:, bass.ds((n * STEP_BLOCKS + bb) * L, L)]

        def bank3(b, inner):
            return ps[:, b, :].rearrange("p (a c) -> p a c", c=inner)

        def head_view(t, hh, width):
            return t[:, :].rearrange("p (a h w) -> p a h w", h=STEP_HEADS, w=width)[:, :, hh, :]

        def hT_of(part, tile, parity, bb):
            v = hT[part][:, bass.ds(tile * (LB * TILE), LB * TILE)].rearrange("p (k t) -> p k t", k=LB)
            at = (parity * STEP_BLOCKS + bb) * P
            return v[:, :, at:at + P]

        def wait_apart(eng, semaphore, value):
            eng.wait_ge(semaphore, value)
            eng.sem_inc(waits_passed, 1)

        def run_steps(eng, step):
            step(0, 0, None)
            with eng.Fori(0, STEPS // 2 - 1) as i:
                step(2 * i + 1, 1, i)
                step(2 * i + 2, 0, i)
            step(STEPS - 1, 1, STEPS // 2 - 1)
            step(STEPS, 0, STEPS // 2 - 1)

        def kinds(n):
            if not isinstance(n, int):
                return True, True, True
            return n < STEPS, n < STEPS - 1, n > 0

        def run_groups(eng, pair):
            with eng.Fori(0, GROUPS // 2 - 1) as i:
                pair(i, False)
            pair(GROUPS // 2 - 1, True)

        def w_source(g, u):
            if u < 2 * CHUNKS:
                c, up = divmod(u, 2)
                return w_gate_up[bass.ds((g * CHUNKS + c) * P + up * INTER, P), :]
            c = u - 2 * CHUNKS
            return w_down[:, bass.ds((g * CHUNKS + c) * P, P)].rearrange("(hb p) i -> p hb i", p=P)

        def prepared(i, k, last):
            second, t = divmod(k, GROUP_UNITS)
            if second:
                if last or t == 0:
                    return []
                t -= 1
            elif t == GROUP_UNITS - 1:
                return []
            return [(2 * i + 1 + second, u, (1 + second) * W_UNITS + u) for u in (2 * t, 2 * t + 1)]

        @block.sync
        def _(sp):
            sp.dma_start(k_loaded, ssm_kernel).then_inc(kp_loaded, 16)
            sp.dma_start(dcol, skip.rearrange("(h o) -> h o", o=1)).then_inc(kp_loaded, 16)

            def load_rows(n):
                for bb in range(STEP_BLOCKS):
                    if not isinstance(n, int) or n > 0:
                        wait_apart(sp, c_transposed, n * STEP_BLOCKS + bb - 1)
                    for q in range(BLOCK_BATCHES):
                        b = bb * BLOCK_BATCHES + q
                        at = slice(q * STEP_ROWS, (q + 1) * STEP_ROWS)
                        sp.dma_start(acc[at, bass.ds((n * STEP_BLOCKS + bb) * L, L)],
                                     x[b, bass.ds(n * STEP_ROWS, STEP_ROWS), :]).then_inc(cx_loaded[bb], 16)
                        sp.dma_start(cnat[at, bb, :],
                                     ctx[b, bass.ds(n * STEP_ROWS, STEP_ROWS), :]).then_inc(cx_loaded[bb], 16)

            def load_toep(n, k):
                g = n * STEP_HEADS + k
                if not isinstance(n, int) or g >= 2:
                    wait_apart(sp, y_ready, (g - 1) * LB)
                src = toeplitz[bass.ds(g, 1), :, :].rearrange("o m x -> (o m) x")
                sp.dma_start(toep[k % 2][:, :], src).then_inc(toep_loaded[k % 2], 16)

            def load_w(g, u, w):
                if not isinstance(g, int) or w >= WNAT:
                    wait_apart(sp, w_transposed, g * W_UNITS + u - WNAT + 1)
                dst = wnat[:, w % WNAT, :]
                if u >= 2 * CHUNKS:
                    dst = dst.rearrange("p (hb i) -> p hb i", i=P)
                sp.dma_start(dst, w_source(g, u)).then_inc(wnat_loaded[w % WNAT], 16)

            load_rows(0)
            for u in range(WNAT):
                load_w(0, u, u)
            sp.wait_ge(kp_ready, 2)
            sp.dma_start(kpad, kp[:, :]).then_inc(kpad_written, 16)
            sp.wait_ge(kpad_written, 16)
            load_toep(0, 0)
            load_toep(0, 1)
            for u in range(WNAT, W_UNITS):
                load_w(0, u, u)

            def step(n, parity, i):
                conv, prep, post = kinds(n)
                if prep:
                    load_rows(n + 1)
                if conv:
                    for k in range(2, 6 if prep else STEP_HEADS):
                        load_toep(n, k)

            run_steps(sp, step)

            def pair(i, last):
                for k in range(1 if last else 2):
                    for u in range(W_UNITS):
                        load_w(2 * i + 1 + k, u, (1 + k) * W_UNITS + u)

            run_groups(sp, pair)
            for t in range(TILES):
                for q in range(TILE_BLOCKS):
                    n, bb = divmod(t * TILE_BLOCKS + q, STEP_BLOCKS)
                    sp.wait_ge(added, D_FREE + (GROUPS - 1) * BLOCKS + t * TILE_BLOCKS + q + 1)
                    for r in range(BLOCK_BATCHES):
                        sp.dma_start(out[bb * BLOCK_BATCHES + r, n * STEP_ROWS:(n + 1) * STEP_ROWS, :],
                                     acc[r * STEP_ROWS:(r + 1) * STEP_ROWS,
                                         (t * TILE_BLOCKS + q) * L:(t * TILE_BLOCKS + q + 1) * L]).then_inc(stored, 16)
            sp.wait_ge(stored, 16 * BLOCKS * BLOCK_BATCHES)

        @block.gpsimd
        def _(pool):
            pool.sem_inc(product_done, GU_FREE)
            pool.sem_inc(a_split, A_FREE)
            pool.sem_inc(d_ready, DOWN_FREE)
            pool.sem_inc(added, D_FREE)
            pool.sem_inc(h_split, H_FREE)
            nc.gpsimd.memset(ident[:, :], 0.0).then_inc(ident_ready, 1)
            nc.gpsimd.memset(flip[:, :], 0.0).then_inc(ident_ready, 1)
            nc.gpsimd.memset(kp[:, L:KROW], 0.0).then_inc(consts_ready, 1)
            nc.gpsimd.memset(minus_half[:, :], -0.5).then_inc(consts_ready, 1)
            pool.wait_ge(ident_ready, 2)
            nc.gpsimd.affine_select(out=ident[:, :], in_=ident[:, :], compare_op=ALU.not_equal, fill=1.0, base=0,
                                    pattern=[[-1, P]], channel_multiplier=1).then_inc(ident_ready, 1)
            nc.gpsimd.affine_select(out=flip[:, :], in_=flip[:, :], compare_op=ALU.not_equal, fill=1.0, base=1 - P,
                                    pattern=[[1, P]], channel_multiplier=1).then_inc(ident_ready, 1)
            pool.wait_ge(consts_ready, 2)

            def inverse_deviation(n, lo, hi):
                wait_apart(pool, aggr_done, n + 1)
                nc.gpsimd.tensor_scalar(vareps[:, lo:hi], meanvar[:, lo:hi, 1], EPS, None,
                                        ALU.add).then_inc(vareps_done, 1)
                pool.wait_ge(vareps_done, n + 1)
                nc.gpsimd.tensor_tensor(rstd[:, lo:hi], vareps[:, lo:hi], minus_half[:, lo:hi],
                                        ALU.pow).then_inc(rstd_ready, 1)

            def pair_products(n, k, parity):
                g = n * STEP_HEADS + k
                if not isinstance(n, int) or g >= 2:
                    pool.wait_ge(y_ready, (g - 1) * LB)
                if k % STEP_HEADS == 0:
                    pool.wait_ge(c_evac, (n + k // STEP_HEADS + 1) * STEP_BLOCKS)
                c = head_view(cT, k % STEP_HEADS, CW)
                o = kv[k % 2][:, :].rearrange("p (a w) -> p a w", w=PAIRS)
                od = o[:, :, 0:DIAG * HD].rearrange("p a (d i) -> p a d i", i=HD)
                step_a = STEP_HEADS * CW
                nc.gpsimd.tensor_tensor(od, _pattern(c, [(step_a, JB), (0, DIAG), (1, HD)]),
                                        _pattern(c, [(step_a, JB), (1, DIAG), (1, HD)]), ALU.mult)
                nc.gpsimd.tensor_tensor(o[:, :, DIAG * HD:PAIRS], c[:, :, 0:DIAG], c[:, :, DIAG:2 * DIAG],
                                        ALU.mult).then_inc(kv_ready, 1)

            inverse_deviation(0, 2, 4)
            pair_products(0, 0, 0)
            pair_products(0, 1, 0)

            def step(n, parity, i):
                conv, prep, post = kinds(n)
                if conv:
                    pair_products(n, 2, parity)
                if prep or post:
                    inverse_deviation(n + 1, 0 if post else 2, 4 if prep else 2)
                if conv:
                    pair_products(n, 3, parity)
                if prep:
                    pair_products(n, 4, 1 - parity)
                    pair_products(n, 5, 1 - parity)

            run_steps(pool, step)

        @block.scalar
        def _(act):
            def evac_y(n, k, parity):
                g = n * STEP_HEADS + k
                for j in range(LB):
                    act.wait_ge(y_ready, g * LB + j + 1)
                    if j == 0 and (not isinstance(n, int) or g >= 2):
                        act.wait_ge(reduced, g - 1)
                    y = ps[:, j, 0:B * PAIRS].rearrange("p (b w) -> p b w", w=PAIRS)
                    o = ysb[k % 2][:, :].rearrange("p (j b w) -> p j b w", b=B, w=YW)[:, j, :, :]
                    yd = y[:, :, 0:DIAG * HD].rearrange("p b (d i) -> p b d i", i=HD)
                    od = o[:, :, 0:DIAG * QW].rearrange("p b (d i) -> p b d i", i=QW)
                    nc.scalar.activation(od[:, :, :, 0:HD], yd, ACT.Copy)
                    nc.scalar.activation(od[:, :, 1:DIAG, HD:QW], yd[:, :, 1:DIAG, :], ACT.Copy)
                    nc.scalar.activation(o[:, :, DIAG * QW:YW], y[:, :, DIAG * HD:PAIRS],
                                         ACT.Copy).then_inc(y_evac, 1)

            def evac_c(n, parity):
                for bb in range(STEP_BLOCKS):
                    act.wait_ge(c_transposed, n * STEP_BLOCKS + bb + 1)
                    if bb == 0 and (not isinstance(n, int) or n > 0):
                        act.wait_ge(kv_ready, n * STEP_HEADS)
                    src = ps[:, 6 + bb, :].rearrange("p (j a i) -> p j a i", j=LB, i=HD)
                    dst = cT[:, :].rearrange("p (j c a w) -> p j c a w", j=LB, c=STEP_BLOCKS, w=CW)[:, :, bb, :, :]
                    nc.scalar.activation(dst[:, :, :, 0:HD], src, ACT.Copy)
                    nc.scalar.activation(dst[:, :, :, HD:CW], src[:, :, :, 0:CW - HD], ACT.Copy).then_inc(c_evac, 1)

            def evac_q(n, parity):
                for bb in range(STEP_BLOCKS):
                    act.wait_ge(q_transposed, n * STEP_BLOCKS + bb + 1)
                    if bb == 0 and (not isinstance(n, int) or n > 1):
                        act.wait_ge(reduced, (n - 1) * STEP_HEADS)
                    src = ps[:, 4 + bb, :].rearrange("p (j a i) -> p j a i", j=LB, i=HD)
                    dst = qT[parity][:, :].rearrange("p (j c a w) -> p j c a w", j=LB, c=STEP_BLOCKS,
                                                     w=QW)[:, :, bb, :, :]
                    nc.scalar.activation(dst[:, :, :, 0:HD], src, ACT.Copy)
                    nc.scalar.activation(dst[:, :, :, HD:QW], src, ACT.Copy).then_inc(q_evac, 1)

            def round_w(g, u, w):
                act.wait_ge(w_transposed, g * W_UNITS + u + 1)
                if u == 0 and w > 0:
                    act.wait_ge(d_ready, DOWN_FREE + (g - 1) * BLOCKS)
                dst = w_slot[(w // W_UNITS) % 2][0][:, u * 512:(u + 1) * 512]
                nc.scalar.activation(dst, ps[:, 6 + w % 2, :], ACT.Copy).then_inc(w_hi, 1)

            evac_c(0, 0)
            evac_q(0, 0)
            for u in range(W_UNITS):
                round_w(0, u, u)

            def step(n, parity, i):
                conv, prep, post = kinds(n)
                for k in range(3 if conv else 0):
                    evac_y(n, k, parity)
                if prep:
                    evac_c(n + 1, 1 - parity)
                    evac_q(n + 1, 1 - parity)
                if conv:
                    evac_y(n, 3, parity)
                if post:
                    for bb in range(STEP_BLOCKS):
                        act.wait_ge(h_transposed, (n - 1) * STEP_BLOCKS + bb + 1)
                        nc.scalar.activation(hT_of(0, i, 1 - parity, bb), bank3(6 + bb, P),
                                             ACT.Copy).then_inc(h_hi, 1)

            run_steps(act, step)

            act.wait_ge(h_split, H_FREE + BLOCKS)

            def pair(i, last):
                for k in range(2 * GROUP_UNITS):
                    u = 2 * GROUP_UNITS * i + k
                    for c in range(CHUNKS):
                        cc = CHUNKS * u + c
                        act.wait_ge(gate_up_ready, cc + 1)
                        act.wait_ge(a_split, cc + 1)
                        nc.scalar.activation(a_full[:, c, :], ps[:, 2 * c, :], ACT.Silu).then_inc(silu_ready, 1)
                        act.wait_ge(product_done, GU_FREE + cc + 1)
                        act.wait_ge(d_ready, (u + 1) * TILE_BLOCKS)
                        nc.scalar.activation(a_part[k % 2][0][:, c * TILE:(c + 1) * TILE], a_full[:, c, :],
                                             ACT.Copy).then_inc(a_hi, 1)
                    for g, wu, w in prepared(i, k, last):
                        round_w(g, wu, w)

            run_groups(act, pair)

        @block.vector
        def _(dve):
            def products(n, k, parity):
                g = n * STEP_HEADS + k
                if k == 0:
                    dve.wait_ge(q_evac, (n + 1) * STEP_BLOCKS)
                if not isinstance(n, int) or g > 0:
                    dve.wait_ge(reduced, g)
                dve.wait_ge(y_evac, (g + 1) * LB)
                y = ysb[k % 2][:, :].rearrange("p (a w) -> p a w", w=YW)
                q = head_view(qT[parity], k, QW)
                p = prod[:, :].rearrange("p (a t i) -> p a t i", t=TERMS, i=HD)
                sq = STEP_HEADS * QW
                nc.vector.tensor_tensor(p[:, :, 0:DIAG, :], _pattern(y, [(YW, JB), (QW, DIAG), (1, HD)]),
                                        _pattern(q, [(sq, JB), (1, DIAG), (1, HD)]),
                                        ALU.mult).then_inc(multiplied, 1)
                nc.vector.tensor_tensor(p[:, :, DIAG + 1:TERMS, :],
                                        _pattern(y, [(YW, JB), (-(QW - 1), DIAG - 1), (1, HD)],
                                                 (DIAG - 1) * QW + HD - (DIAG - 1)),
                                        _pattern(q, [(sq, JB), (1, DIAG - 1), (1, HD)], HD - (DIAG - 1)),
                                        ALU.mult).then_inc(multiplied, 1)
                nc.vector.tensor_tensor(p[:, :, DIAG, :].rearrange("p a (c i) -> p a c i", c=2),
                                        _pattern(y, [(YW, JB), (0, 2), (1, DIAG)], DIAG * QW),
                                        _pattern(q, [(sq, JB), (DIAG, 2), (1, DIAG)], DIAG),
                                        ALU.mult).then_inc(multiplied, 1)
                dve.wait_ge(multiplied, 3 * (g + 1))
                o = oT[parity][:, :].rearrange("p (a h i) -> p a h i", h=STEP_HEADS, i=HD)[:, :, k, :]
                nc.vector.tensor_reduce(o, p.rearrange("p a t i -> p a i t"), AX_X, ALU.add).then_inc(reduced, 1)

            def statistics(at, source, count):
                nc.vector.bn_stats(stats[:, at, :], source).then_inc(stats_done, 1)

            def normalise(at, dst, source, done):
                nc.vector.tensor_scalar(dst, source, meanvar[:, at, 0:1], rstd[:, at:at + 1], ALU.subtract,
                                        ALU.mult).then_inc(done, 1)

            def normalise_query(n, bb):
                normalise(2 + bb, _pattern(normed[:, bb, :], [(P, LB), (-1, P)], P - 1),
                          acc_of(n, bb).rearrange("p (j x) -> p j x", j=LB), q_normed)

            def aggregate(lo, hi, statistics_before, last_inc):
                wait_apart(dve, stats_done, statistics_before)
                for at in range(lo, hi):
                    ins = nc.vector.bn_aggr(meanvar[:, at, :], stats[:, at, :])
                ins.then_inc(aggr_done, 1)

            dve.wait_ge(kp_loaded, 32)
            dve.wait_ge(consts_ready, 2)
            nc.vector.tensor_copy(_pattern(kp, [(-1, L)], L - 1), k_loaded).then_inc(kp_ready, 1)
            dve.wait_ge(kp_ready, 1)
            nc.vector.tensor_tensor(kp[:, L - 1:L], kp[:, L - 1:L], dcol, ALU.add).then_inc(kp_ready, 1)

            def split_w(g, u, w):
                dve.wait_ge(w_hi, g * W_UNITS + u + 1)
                hi, lo = (part[:, u * 512:(u + 1) * 512] for part in w_slot[(w // W_UNITS) % 2])
                nc.vector.tensor_tensor(lo, ps[:, 6 + w % 2, :], hi.bitcast(F32),
                                        ALU.subtract).then_inc(w_split, 1)

            for bb in range(STEP_BLOCKS):
                dve.wait_ge(cx_loaded[bb], 16 * 2 * BLOCK_BATCHES)
                statistics(2 + bb, acc_of(0, bb), None)
            aggregate(2, 4, STEP_BLOCKS, None)
            dve.wait_ge(rstd_ready, 1)
            for bb in range(STEP_BLOCKS):
                normalise_query(0, bb)
            for u in range(W_UNITS):
                split_w(0, u, u)

            def step(n, parity, i):
                conv, prep, post = kinds(n)
                if conv:
                    products(n, 0, parity)
                if post:
                    for bb in range(STEP_BLOCKS):
                        dve.wait_ge(o_transposed, (n - 1) * STEP_BLOCKS + bb + 1)
                        nc.vector.tensor_tensor(acc_of(n - 1, bb), ps[:, 4 + bb, :], acc_of(n - 1, bb),
                                                ALU.add).then_inc(o_added, 1)
                if prep:
                    for bb in range(STEP_BLOCKS):
                        wait_apart(dve, cx_loaded[bb], (n + 2) * (16 * 2 * BLOCK_BATCHES))
                        statistics(2 + bb, acc_of(n + 1, bb), None)
                if post:
                    wait_apart(dve, o_added, n * STEP_BLOCKS)
                    for bb in range(STEP_BLOCKS):
                        statistics(bb, acc_of(n - 1, bb), None)
                if prep or post:
                    done = (n + 2) * STEP_BLOCKS + n * STEP_BLOCKS if prep else (STEPS + n) * STEP_BLOCKS
                    aggregate(0 if post else 2, 4 if prep else 2, done, None)
                if conv:
                    products(n, 1, parity)
                dve.wait_ge(rstd_ready, n + 2)
                if prep:
                    for bb in range(STEP_BLOCKS):
                        dve.wait_ge(q_transposed, n * STEP_BLOCKS + bb + 1)
                        normalise_query(n + 1, bb)
                if conv:
                    products(n, 2, parity)
                if post:
                    for bb in range(STEP_BLOCKS):
                        if prep:
                            dve.wait_ge(q_transposed, (n + 1) * STEP_BLOCKS + bb + 1)
                        normalise(bb, normed[:, bb, :], acc_of(n - 1, bb), h_normed)
                if conv:
                    products(n, 3, parity)
                if post:
                    for bb in range(STEP_BLOCKS):
                        dve.wait_ge(h_hi, (n - 1) * STEP_BLOCKS + bb + 1)
                        nc.vector.tensor_tensor(hT_of(1, i, 1 - parity, bb), bank3(6 + bb, P),
                                                hT_of(0, i, 1 - parity, bb).bitcast(F32),
                                                ALU.subtract).then_inc(h_split, 1)

            run_steps(dve, step)

            def add_down(u, t):
                for q in range(TILE_BLOCKS):
                    d = TILE_BLOCKS * u + q
                    dve.wait_ge(d_ready, DOWN_FREE + d + 1)
                    a = acc[:, (t * TILE_BLOCKS + q) * L:(t * TILE_BLOCKS + q + 1) * L]
                    nc.vector.tensor_tensor(a, ps[:, 4 + q % 2, :], a, ALU.add).then_inc(added, 1)

            def pair(i, last):
                for k in range(2 * GROUP_UNITS):
                    u = 2 * GROUP_UNITS * i + k
                    for c in range(CHUNKS):
                        cc = CHUNKS * u + c
                        dve.wait_ge(silu_ready, cc + 1)
                        nc.vector.tensor_tensor(a_full[:, c, :], ps[:, 2 * c + 1, :], a_full[:, c, :],
                                                ALU.mult).then_inc(product_done, 1)
                        dve.wait_ge(a_hi, cc + 1)
                        hi, lo = (part[:, c * TILE:(c + 1) * TILE] for part in a_part[k % 2])
                        nc.vector.tensor_tensor(lo, a_full[:, c, :], hi.bitcast(F32),
                                                ALU.subtract).then_inc(a_split, 1)
                    if k > 0:
                        add_down(u - 1, (k - 1) % GROUP_UNITS)
                    for g, wu, w in prepared(i, k, last):
                        split_w(g, wu, w)
                add_down(u, GROUP_UNITS - 1)

            run_groups(dve, pair)

        @block.tensor
        def _(pe):
            def transposes(b, source, done, permutation=ident):
                for j in range(4):
                    ins = nc.tensor.transpose(ps[:, b, j * P:(j + 1) * P], source(j), permutation[:, :])
                ins.then_inc(done, 1)

            def transpose_c(n):
                for bb in range(STEP_BLOCKS):
                    pe.wait_ge(cx_loaded[bb], (n + 1) * (16 * 2 * BLOCK_BATCHES))
                    if not isinstance(n, int) or n > 0:
                        pe.wait_ge(c_evac, (n - 1) * STEP_BLOCKS + bb + 1)
                        pe.wait_ge(h_split, H_FREE + (n - 3) * STEP_BLOCKS + bb + 1 if not isinstance(n, int) or n > 1
                                   else H_FREE)
                    transposes(6 + bb, lambda j: cnat[:, bb, j * P:(j + 1) * P], c_transposed)

            def transpose_q(n):
                for bb in range(STEP_BLOCKS):
                    pe.wait_ge(q_normed, n * STEP_BLOCKS + bb + 1)
                    if not isinstance(n, int) or n > 0:
                        pe.wait_ge(q_evac, (n - 1) * STEP_BLOCKS + bb + 1)
                    if not isinstance(n, int) or n > 1:
                        pe.wait_ge(o_added, (n - 2) * STEP_BLOCKS + bb + 1)
                    transposes(4 + bb, lambda j: normed[:, bb, j * P:(j + 1) * P], q_transposed)

            def transpose_w(g, u, w):
                pe.wait_ge(wnat_loaded[w % WNAT], 16 * (w // WNAT + 1) if isinstance(g, int) and g == 0 else
                           16 * ((g - w // W_UNITS) * W_UNITS // WNAT + w // WNAT + 1) if isinstance(g, int) else
                           (g - w // W_UNITS) * (16 * W_UNITS // WNAT) + 16 * (w // WNAT + 1))
                if isinstance(g, int) and w < 2:
                    pe.wait_ge(c_evac, w + 1)
                else:
                    pe.wait_ge(w_split, g * W_UNITS + u - 1)
                transposes(6 + w % 2, lambda j: wnat[:, w % WNAT, j * P:(j + 1) * P], w_transposed)

            def convolve(n, k, parity):
                g = n * STEP_HEADS + k
                pe.wait_ge(toep_loaded[k % 2], (g - k % 2) * 8 + 16)
                pe.wait_ge(kv_ready, g + 1)
                for j in range(LB):
                    if not isinstance(n, int) or g > 0:
                        pe.wait_ge(y_evac, (g - 1) * LB + j + 1)
                    for d in range(j + 1):
                        src = kv[k % 2][:, (j - d) * B * PAIRS:(j - d + 1) * B * PAIRS]
                        ins = nc.tensor.matmul(ps[:, j, 0:B * PAIRS], toep[k % 2][:, (LB - 1 - d) * P:(LB - d) * P], src,
                                               start=d == 0, stop=d == j)
                    ins.then_inc(y_ready, 1)

            pe.wait_ge(ident_ready, 4)
            transpose_c(0)
            transpose_q(0)
            for u in range(W_UNITS):
                transpose_w(0, u, u)

            def step(n, parity, i):
                conv, prep, post = kinds(n)
                if conv:
                    convolve(n, 0, parity)
                if post:
                    pe.wait_ge(reduced, n * STEP_HEADS)
                    for bb in range(STEP_BLOCKS):
                        if prep or conv:
                            pe.wait_ge(q_evac, n * STEP_BLOCKS + bb + 1)
                        else:
                            pe.wait_ge(o_added, (n - 2) * STEP_BLOCKS + bb + 1)
                        transposes(4 + bb, lambda j: oT[1 - parity][:, (j * B + bb * BLOCK_BATCHES) * STEP_ROWS:
                                                                    (j * B + bb * BLOCK_BATCHES) * STEP_ROWS + P],
                                   o_transposed, flip)
                if conv:
                    convolve(n, 1, parity)
                if prep:
                    if isinstance(n, int) and n == 0:
                        pe.wait_ge(w_split, W_UNITS)
                    transpose_c(n + 1)
                if conv:
                    convolve(n, 2, parity)
                if prep:
                    transpose_q(n + 1)
                if conv:
                    convolve(n, 3, parity)
                if post:
                    for bb in range(STEP_BLOCKS):
                        pe.wait_ge(h_normed, (n - 1) * STEP_BLOCKS + bb + 1)
                        if prep:
                            pe.wait_ge(c_evac, (n + 1) * STEP_BLOCKS + bb + 1)
                        else:
                            pe.wait_ge(h_split, H_FREE + (n - 2) * STEP_BLOCKS + bb + 1)
                        transposes(6 + bb, lambda j: normed[:, bb, j * P:(j + 1) * P], h_transposed)

            run_steps(pe, step)

            pe.wait_ge(h_split, H_FREE + BLOCKS)

            def gate_up(u, k):
                slot, t = divmod(k, GROUP_UNITS)
                for c in range(CHUNKS):
                    cc = CHUNKS * u + c
                    pe.wait_ge(product_done, cc + 1)
                    for up in range(2):
                        for j in range(LB):
                            for n, (a, b) in enumerate(PARTS):
                                at = (2 * c + up) * 512 + j * P
                                ins = nc.tensor.matmul(
                                    ps[:, 2 * c + up, :], w_slot[slot][a][:, at:at + P],
                                    hT[b][:, (t * LB + j) * TILE:(t * LB + j + 1) * TILE],
                                    start=j == 0 and n == 0, stop=j == LB - 1 and n == 2)
                    ins.then_inc(gate_up_ready, 1)

            def down(u, k):
                slot = k // GROUP_UNITS
                pe.wait_ge(a_split, CHUNKS * (u + 1) + A_FREE)
                for q in range(TILE_BLOCKS):
                    pe.wait_ge(added, TILE_BLOCKS * u + q + 1)
                    for c in range(CHUNKS):
                        for n, (a, b) in enumerate(PARTS):
                            ins = nc.tensor.matmul(
                                ps[:, 4 + q % 2, :], a_part[k % 2][a][:, c * TILE + q * P:c * TILE + (q + 1) * P],
                                w_slot[slot][b][:, (2 * CHUNKS + c) * 512:(2 * CHUNKS + c + 1) * 512],
                                start=c == 0 and n == 0, stop=c == CHUNKS - 1 and n == 2)
                    ins.then_inc(d_ready, 1)

            def pair(i, last):
                for k in range(2 * GROUP_UNITS):
                    u = 2 * GROUP_UNITS * i + k
                    if k % GROUP_UNITS == 0:
                        pe.wait_ge(w_split, (2 * i + k // GROUP_UNITS + 1) * W_UNITS)
                    gate_up(u, k)
                    if k > 0:
                        down(u - 1, k - 1)
                    for g, wu, w in prepared(i, k, last):
                        transpose_w(g, wu, w)
                down(u, k)

            run_groups(pe, pair)


def _pattern(ap, pattern, offset=0):
    return bass.AP(tensor=ap.tensor, offset=ap.offset + offset, ap=[list(ap.ap[0])] + [list(q) for q in pattern])


_INS = ["x", "ctx_2048", "L0_xattn_ssm_kernel", "L0_xattn_D", "L0_ffn_w_gate_up", "L0_ffn_w_down"]


def kernel(**inputs):
    import numpy as _np
    import concourse.bacc as _bacc
    from concourse import mybir as _mybir
    from concourse.bass_utils import run_bass_kernel_spmd as _run

    nc = _bacc.Bacc("TRN2", target_bir_lowering=False, num_devices=1)
    arrays, args = {}, []
    for name in _INS:
        a = _np.ascontiguousarray(inputs[name])
        arrays[f"in_{name}"] = a
        args.append(nc.dram_tensor(f"in_{name}", a.shape, _mybir.dt.from_np(a.dtype), kind="ExternalInput").ap())
    shape = inputs["x"].shape
    result = nc.dram_tensor("out_0", shape, _mybir.dt.float32, kind="ExternalOutput").ap()
    xattn_ffn(nc, *args, result)
    r = _run(nc, [arrays], core_ids=[0])
    return r.results[0]["out_0"]
```

```python
from contextlib import ExitStack

import concourse.bass as bass
from concourse import mybir

P = 128
ALU = mybir.AluOpType
ACT = mybir.ActivationFunctionType
F32 = mybir.dt.float32
F32R = mybir.dt.float32r
AX_X = mybir.AxisListType.X
EPS = 1e-5


def xattn_ffn(nc, x, ctx, ssm_kernel, skip, w_gate_up, w_down, out):
    B, S, L = x.shape
    H = ssm_kernel.shape[0]
    HD = S // H
    INTER = w_down.shape[1]
    LB = L // P
    STEP_HEADS = 4
    STEP_ROWS = STEP_HEADS * HD
    STEPS = H // STEP_HEADS
    BLOCK_BATCHES = P // STEP_ROWS
    STEP_BLOCKS = B // BLOCK_BATCHES
    BLOCKS = STEPS * STEP_BLOCKS
    TILE_BLOCKS = 4
    TILES = BLOCKS // TILE_BLOCKS
    TILE = TILE_BLOCKS * P
    DIAG = HD // 2
    PAIRS = DIAG * HD + DIAG
    CW = HD + DIAG
    QW = 2 * HD
    YW = DIAG * 2 * HD + DIAG
    TERMS = HD
    JB = LB * B
    PAD = P - 1
    CHUNKS = 2
    GROUPS = INTER // (CHUNKS * P)
    W_UNITS = 3 * CHUNKS
    WNAT = 4
    GROUP_UNITS = TILES
    assert (LB, STEPS, STEP_BLOCKS, TILES, DIAG) == (4, 8, 2, 4, 4)
    PARTS = ((0, 0), (0, 1), (1, 0))

    KROW = PAD + L + 1
    kpad_dram = nc.dram_tensor("kpad", (H, KROW), F32)
    kpad = kpad_dram.ap()
    toeplitz = bass.AP(tensor=kpad_dram, offset=0, ap=[[KROW, H], [1, P], [1, L]])

    with ExitStack() as stack:
        def sb(name, shape, dt=F32, where=stack):
            return where.enter_context(nc.sbuf_tensor(name, shape, dt))

        def sem(name):
            return stack.enter_context(nc.semaphore(name))

        ident = sb("ident", [P, P])
        flip = sb("flip", [P, P])
        acc = sb("acc", [P, BLOCKS * L])
        hT = [sb("hT_hi", [P, TILES * LB * TILE], F32R), sb("hT_lo", [P, TILES * LB * TILE], F32R)]
        w_slot = [[sb("w0_hi", [P, W_UNITS * 512], F32R), sb("w0_lo", [P, W_UNITS * 512], F32R)]]
        stats = sb("stats", [P, 4, 6])
        meanvar = sb("meanvar", [P, 4, 2])
        vareps = sb("vareps", [P, 4])
        rstd = sb("rstd", [P, 4])
        minus_half = sb("minus_half", [P, 4])

        phase_a = ExitStack()
        with phase_a:
            kv = [sb(f"kv{i}", [P, JB * PAIRS], F32, phase_a) for i in range(2)]
            toep = [sb(f"toep{i}", [P, L], F32, phase_a) for i in range(2)]
            cT = sb("cT", [P, JB * STEP_HEADS * CW], F32, phase_a)
            cnat = sb("cnat", [P, 2, L], F32, phase_a)
            qn = sb("qn", [P, 2, L], F32, phase_a)
            hn = sb("hn", [P, 2, L], F32, phase_a)
            qT = [sb(f"qT{i}", [P, JB * STEP_HEADS * QW], F32, phase_a) for i in range(2)]
            ysb = [sb(f"ysb{i}", [P, JB * YW], F32, phase_a) for i in range(2)]
            prod = [sb(f"prod{i}", [P, JB * TERMS * HD], F32, phase_a) for i in range(2)]
            oT = sb("oT", [P, JB * STEP_ROWS], F32, phase_a)
        kp = prod[0][0:H, 0:KROW]
        k_loaded = prod[0][0:H, KROW:KROW + L]
        dcol = prod[0][0:H, KROW + L:KROW + L + 1]
        a_part = [[sb(f"a{i}_{n}", [P, CHUNKS * TILE], F32R) for n in ("hi", "lo")] for i in range(2)]
        a_full = sb("a_full", [P, 2, TILE])
        wnat_first = [qT[1][:, k * 512:(k + 1) * 512] for k in range(4)] + [hn[:, k, :] for k in range(2)]
        wnat_later = sb("wnat", [P, WNAT, 512])
        w_slot.append([sb("w1_hi", [P, W_UNITS * 512], F32R), sb("w1_lo", [P, W_UNITS * 512], F32R)])

        ps = stack.enter_context(nc.psum_tensor("ps", [P, 8, 512], F32))

        waits_passed = sem("waits_passed")
        ident_ready = sem("ident_ready")
        consts_ready = sem("consts_ready")
        kp_loaded = sem("kp_loaded")
        kp_ready = sem("kp_ready")
        kpad_written = sem("kpad_written")
        first_c_loaded = [sem(f"first_c_loaded{i}") for i in range(2)]
        cx_loaded = [sem(f"cx_loaded{i}") for i in range(2)]
        toep_loaded = [sem(f"toep_loaded{i}") for i in range(2)]
        stats_done = sem("stats_done")
        vareps_done = sem("vareps_done")
        aggr_done = sem("aggr_done")
        rstd_ready = sem("rstd_ready")
        q_normed = sem("q_normed")
        h_normed = sem("h_normed")
        c_transposed = sem("c_transposed")
        q_transposed = sem("q_transposed")
        o_transposed = sem("o_transposed")
        h_transposed = sem("h_transposed")
        c_evac = sem("c_evac")
        q_evac = sem("q_evac")
        kv_ready = sem("kv_ready")
        y_ready = sem("y_ready")
        y_evac = sem("y_evac")
        multiplied = sem("multiplied")
        mirrored = sem("mirrored")
        reduced = sem("reduced")
        o_added = sem("o_added")
        h_hi = sem("h_hi")
        h_split = sem("h_split")
        first_loaded = [sem(f"first_loaded{i}") for i in range(W_UNITS)]
        wnat_loaded = [sem(f"wnat_loaded{i}") for i in range(WNAT)]
        w_transposed = sem("w_transposed")
        w_hi = sem("w_hi")
        w_split = sem("w_split")
        gate_up_ready = sem("gate_up_ready")
        silu_ready = sem("silu_ready")
        product_done = sem("product_done")
        a_hi = sem("a_hi")
        a_split = sem("a_split")
        d_ready = sem("d_ready")
        added = sem("added")
        stored = sem("stored")
        GU_FREE, A_FREE, D_FREE, H_FREE = 2, 2, 2, 2
        DOWN_FREE = 2 * TILE_BLOCKS

        block = stack.enter_context(nc.Block())

        def rows(dram, n, bb):
            return dram[bb * BLOCK_BATCHES:(bb + 1) * BLOCK_BATCHES, bass.ds(n * STEP_ROWS, STEP_ROWS), :]

        def acc_of(n, bb):
            return acc[:, bass.ds((n * STEP_BLOCKS + bb) * L, L)]

        def bank3(b, inner):
            return ps[:, b, :].rearrange("p (a c) -> p a c", c=inner)

        def head_view(t, hh, width):
            return t[:, :].rearrange("p (a h w) -> p a h w", h=STEP_HEADS, w=width)[:, :, hh, :]

        def hT_of(part, tile, parity, bb):
            v = hT[part][:, bass.ds(tile * (LB * TILE), LB * TILE)].rearrange("p (k t) -> p k t", k=LB)
            at = (parity * STEP_BLOCKS + bb) * P
            return v[:, :, at:at + P]

        def wait_apart(eng, semaphore, value):
            eng.wait_ge(semaphore, value)
            eng.sem_inc(waits_passed, 1)

        def run_steps(eng, step):
            step(0, 0, None)
            with eng.Fori(0, STEPS // 2 - 1) as i:
                step(2 * i + 1, 1, i)
                step(2 * i + 2, 0, i)
            step(STEPS - 1, 1, STEPS // 2 - 1)
            step(STEPS, 0, STEPS // 2 - 1)

        def kinds(n):
            if not isinstance(n, int):
                return True, True, True
            return n < STEPS, n < STEPS - 1, n > 0

        def run_groups(eng, pair):
            with eng.Fori(0, GROUPS // 2 - 1) as i:
                pair(i, False)
            pair(GROUPS // 2 - 1, True)

        def w_source(g, u):
            if u < 2 * CHUNKS:
                c, up = divmod(u, 2)
                return w_gate_up[bass.ds((g * CHUNKS + c) * P + up * INTER, P), :]
            c = u - 2 * CHUNKS
            return w_down[:, bass.ds((g * CHUNKS + c) * P, P)].rearrange("(hb p) i -> p hb i", p=P)

        def first_weights(n, k):
            return ((0, 1, 2, 3), (4, 5), (), ())[k] if isinstance(n, int) and n == 0 else ()

        def w_bank(w):
            return (6, 7, 4, 5, 4, 5)[w] if w < W_UNITS else 6 + w % 2

        def prepared(i, k, last):
            second, t = divmod(k, GROUP_UNITS)
            if t == 0 or (second and last):
                return []
            return [(2 * i + 1 + second, u, (1 + second) * W_UNITS + u) for u in (2 * t - 2, 2 * t - 1)]

        @block.sync
        def _(sp):
            for bb in range(STEP_BLOCKS):
                sp.dma_start(cnat[:, bb, :], rows(ctx, 0, bb)).then_inc(first_c_loaded[bb], 16)
            sp.dma_start(k_loaded, ssm_kernel).then_inc(kp_loaded, 16)
            sp.dma_start(dcol, skip.rearrange("(h o) -> h o", o=1)).then_inc(kp_loaded, 16)
            for bb in range(STEP_BLOCKS):
                sp.dma_start(acc_of(0, bb), rows(x, 0, bb)).then_inc(cx_loaded[bb], 16)

            def load_rows(n):
                if isinstance(n, int) and n == 1:
                    sp.wait_ge(stats_done, STEP_BLOCKS)
                for bb in range(STEP_BLOCKS):
                    wait_apart(sp, c_transposed, n * STEP_BLOCKS + bb - 1)
                    sp.dma_start(cnat[:, bb, :], rows(ctx, n, bb)).then_inc(cx_loaded[bb], 16)
                    sp.dma_start(acc_of(n, bb), rows(x, n, bb)).then_inc(cx_loaded[bb], 16)

            def load_toep(n, k):
                g = n * STEP_HEADS + k
                if not isinstance(n, int) or g >= 2:
                    wait_apart(sp, y_ready, (g - 1) * LB)
                src = toeplitz[bass.ds(g, 1), :, :].rearrange("o m x -> (o m) x")
                sp.dma_start(toep[k % 2][:, :], src).then_inc(toep_loaded[k % 2], 16)

            def load_w(g, u, w):
                if w < W_UNITS:
                    dst, loaded = wnat_first[w], first_loaded[w]
                else:
                    wait_apart(sp, w_transposed, g * W_UNITS + u - WNAT + 1)
                    slot = (w - W_UNITS) % WNAT
                    dst, loaded = wnat_later[:, slot, :], wnat_loaded[slot]
                if u >= 2 * CHUNKS:
                    dst = dst.rearrange("p (hb i) -> p hb i", i=P)
                sp.dma_start(dst, w_source(g, u)).then_inc(loaded, 16)

            sp.wait_ge(kp_ready, 2)
            sp.dma_start(kpad, kp[:, :]).then_inc(kpad_written, 16)
            for u in range(2):
                load_w(0, u, u)
            sp.wait_ge(kpad_written, 16)
            load_toep(0, 0)
            for u in range(2, W_UNITS):
                load_w(0, u, u)
            load_toep(0, 1)

            def step(n, parity, i):
                conv, prep, post = kinds(n)
                if prep:
                    load_rows(n + 1)
                if conv:
                    for k in range(2, 6 if prep else STEP_HEADS):
                        load_toep(n, k)

            run_steps(sp, step)

            sp.wait_ge(h_split, H_FREE + BLOCKS)

            def pair(i, last):
                for k in range(1 if last else 2):
                    for u in range(W_UNITS):
                        load_w(2 * i + 1 + k, u, (1 + k) * W_UNITS + u)

            run_groups(sp, pair)
            for t in range(TILES):
                for q in range(TILE_BLOCKS):
                    n, bb = divmod(t * TILE_BLOCKS + q, STEP_BLOCKS)
                    sp.wait_ge(added, D_FREE + (GROUPS - 1) * BLOCKS + t * TILE_BLOCKS + q + 1)
                    sp.dma_start(rows(out, n, bb), acc_of(n, bb)).then_inc(stored, 16)
            sp.wait_ge(stored, 16 * BLOCKS)

        @block.gpsimd
        def _(pool):
            pool.sem_inc(product_done, GU_FREE)
            pool.sem_inc(a_split, A_FREE)
            pool.sem_inc(d_ready, DOWN_FREE)
            pool.sem_inc(added, D_FREE)
            pool.sem_inc(h_split, H_FREE)
            nc.gpsimd.memset(ident[:, :], 0.0).then_inc(ident_ready, 1)
            nc.gpsimd.memset(flip[:, :], 0.0).then_inc(ident_ready, 1)
            nc.gpsimd.memset(kp[:, L:KROW], 0.0).then_inc(consts_ready, 1)
            nc.gpsimd.memset(minus_half[:, :], -0.5).then_inc(consts_ready, 1)
            pool.wait_ge(ident_ready, 2)
            nc.gpsimd.affine_select(out=ident[:, :], in_=ident[:, :], compare_op=ALU.not_equal, fill=1.0, base=0,
                                    pattern=[[-1, P]], channel_multiplier=1).then_inc(ident_ready, 1)
            nc.gpsimd.affine_select(out=flip[:, :], in_=flip[:, :], compare_op=ALU.not_equal, fill=1.0, base=1 - P,
                                    pattern=[[1, P]], channel_multiplier=1).then_inc(ident_ready, 1)
            pool.wait_ge(consts_ready, 2)

            def inverse_deviation(n, lo, hi):
                wait_apart(pool, aggr_done, n + 1)
                nc.gpsimd.tensor_scalar(vareps[:, lo:hi], meanvar[:, lo:hi, 1], EPS, None,
                                        ALU.add).then_inc(vareps_done, 1)
                pool.wait_ge(vareps_done, n + 1)
                nc.gpsimd.tensor_tensor(rstd[:, lo:hi], vareps[:, lo:hi], minus_half[:, lo:hi],
                                        ALU.pow).then_inc(rstd_ready, 1)

            def pair_products(n, k, parity):
                g = n * STEP_HEADS + k
                if not isinstance(n, int) or g >= 2:
                    pool.wait_ge(y_ready, (g - 1) * LB)
                if k % STEP_HEADS == 0:
                    pool.wait_ge(c_evac, (n + k // STEP_HEADS + 1) * STEP_BLOCKS)
                c = head_view(cT, k % STEP_HEADS, CW)
                o = kv[k % 2][:, :].rearrange("p (a w) -> p a w", w=PAIRS)
                od = o[:, :, 0:DIAG * HD].rearrange("p a (d i) -> p a d i", i=HD)
                step_a = STEP_HEADS * CW
                nc.gpsimd.tensor_tensor(od, _pattern(c, [(step_a, JB), (0, DIAG), (1, HD)]),
                                        _pattern(c, [(step_a, JB), (1, DIAG), (1, HD)]), ALU.mult)
                nc.gpsimd.tensor_tensor(o[:, :, DIAG * HD:PAIRS], c[:, :, 0:DIAG], c[:, :, DIAG:2 * DIAG],
                                        ALU.mult).then_inc(kv_ready, 1)

            def mirror_products(n, k, parity):
                g = n * STEP_HEADS + k
                if not isinstance(n, int) or g > 1:
                    pool.wait_ge(reduced, g - 1)
                if k == 0:
                    pool.wait_ge(q_evac, (n + 1) * STEP_BLOCKS)
                pool.wait_ge(y_evac, (g + 1) * LB)
                y = ysb[k % 2][:, :].rearrange("p (a w) -> p a w", w=YW)
                q = head_view(qT[parity], k, QW)
                p = prod[k % 2][:, :].rearrange("p (a t i) -> p a t i", t=TERMS, i=HD)
                nc.gpsimd.tensor_tensor(p[:, :, DIAG + 1:TERMS, :],
                                        _pattern(y, [(YW, JB), (-(QW - 1), DIAG - 1), (1, HD)],
                                                 (DIAG - 1) * QW + HD - (DIAG - 1)),
                                        _pattern(q, [(STEP_HEADS * QW, JB), (1, DIAG - 1), (1, HD)],
                                                 HD - (DIAG - 1)), ALU.mult).then_inc(mirrored, 1)

            pair_products(0, 0, 0)
            inverse_deviation(0, 2, 4)
            pair_products(0, 1, 0)

            def step(n, parity, i):
                conv, prep, post = kinds(n)
                for k in range(STEP_HEADS if conv else 0):
                    if k == 2:
                        inverse_deviation(n + 1, 0 if post else 2, 4 if prep else 2)
                    if k < 2 or prep:
                        pair_products(n, k + 2, parity)
                    mirror_products(n, k, parity)
                if not conv:
                    inverse_deviation(n + 1, 0, 2)

            run_steps(pool, step)

        @block.scalar
        def _(act):
            def evac_y(n, k, parity):
                g = n * STEP_HEADS + k
                for j in range(LB):
                    act.wait_ge(y_ready, g * LB + j + 1)
                    if j == 0 and (not isinstance(n, int) or g >= 2):
                        act.wait_ge(multiplied, 2 * (g - 1))
                        act.wait_ge(mirrored, g - 1)
                    y = ps[:, j, 0:B * PAIRS].rearrange("p (b w) -> p b w", w=PAIRS)
                    o = ysb[k % 2][:, :].rearrange("p (j b w) -> p j b w", b=B, w=YW)[:, j, :, :]
                    yd = y[:, :, 0:DIAG * HD].rearrange("p b (d i) -> p b d i", i=HD)
                    od = o[:, :, 0:DIAG * QW].rearrange("p b (d i) -> p b d i", i=QW)
                    nc.scalar.activation(od[:, :, :, 0:HD], yd, ACT.Copy)
                    nc.scalar.activation(od[:, :, 1:DIAG, HD:QW], yd[:, :, 1:DIAG, :], ACT.Copy)
                    nc.scalar.activation(o[:, :, DIAG * QW:YW], y[:, :, DIAG * HD:PAIRS],
                                         ACT.Copy).then_inc(y_evac, 1)

            def evac_c(n, parity):
                for bb in range(STEP_BLOCKS):
                    act.wait_ge(c_transposed, n * STEP_BLOCKS + bb + 1)
                    if bb == 0 and (not isinstance(n, int) or n > 0):
                        act.wait_ge(kv_ready, n * STEP_HEADS)
                    src = ps[:, 6 + bb, :].rearrange("p (j a i) -> p j a i", j=LB, i=HD)
                    dst = cT[:, :].rearrange("p (j c a w) -> p j c a w", j=LB, c=STEP_BLOCKS, w=CW)[:, :, bb, :, :]
                    nc.scalar.activation(dst[:, :, :, 0:HD], src, ACT.Copy)
                    nc.scalar.activation(dst[:, :, :, HD:CW], src[:, :, :, 0:CW - HD], ACT.Copy).then_inc(c_evac, 1)

            def evac_q(n, parity):
                for bb in range(STEP_BLOCKS):
                    act.wait_ge(q_transposed, n * STEP_BLOCKS + bb + 1)
                    if bb == 0 and (not isinstance(n, int) or n > 1):
                        act.wait_ge(reduced, (n - 1) * STEP_HEADS)
                    src = ps[:, 4 + bb, :].rearrange("p (j a i) -> p j a i", j=LB, i=HD)
                    dst = qT[parity][:, :].rearrange("p (j c a w) -> p j c a w", j=LB, c=STEP_BLOCKS,
                                                     w=QW)[:, :, bb, :, :]
                    nc.scalar.activation(dst[:, :, :, 0:HD], src, ACT.Copy)
                    nc.scalar.activation(dst[:, :, :, HD:QW], src, ACT.Copy).then_inc(q_evac, 1)

            def round_w(g, u, w):
                act.wait_ge(w_transposed, g * W_UNITS + u + 1)
                if u == 0 and w > 0:
                    act.wait_ge(d_ready, DOWN_FREE + (g - 1) * BLOCKS)
                dst = w_slot[(w // W_UNITS) % 2][0][:, u * 512:(u + 1) * 512]
                nc.scalar.activation(dst, ps[:, w_bank(w), :], ACT.Copy).then_inc(w_hi, 1)

            evac_c(0, 0)

            def step(n, parity, i):
                conv, prep, post = kinds(n)
                for k in range(3 if conv else 0):
                    evac_y(n, k, parity)
                    if isinstance(n, int) and n == k == 0:
                        evac_q(0, 0)
                    for u in first_weights(n, k):
                        round_w(0, u, u)
                if not conv:
                    activate(0, 0, 0)
                if prep:
                    evac_c(n + 1, 1 - parity)
                if conv:
                    evac_y(n, 3, parity)
                if prep:
                    evac_q(n + 1, 1 - parity)
                if post:
                    for bb in range(STEP_BLOCKS):
                        act.wait_ge(h_transposed, (n - 1) * STEP_BLOCKS + bb + 1)
                        nc.scalar.activation(hT_of(0, i, 1 - parity, bb), bank3(6 + bb, P),
                                             ACT.Copy).then_inc(h_hi, 1)

            def activate(u, k, c):
                cc = CHUNKS * u + c
                act.wait_ge(gate_up_ready, cc + 1)
                act.wait_ge(a_split, cc + 1)
                nc.scalar.activation(a_full[:, c, :], ps[:, 2 * c, :], ACT.Silu).then_inc(silu_ready, 1)
                act.wait_ge(product_done, GU_FREE + cc + 1)
                act.wait_ge(d_ready, (u + 1) * TILE_BLOCKS)
                nc.scalar.activation(a_part[k % 2][0][:, c * TILE:(c + 1) * TILE], a_full[:, c, :],
                                     ACT.Copy).then_inc(a_hi, 1)

            run_steps(act, step)
            activate(0, 0, 1)

            def pair(i, last):
                for k in range(1, 2 * GROUP_UNITS + (not last)):
                    for c in range(CHUNKS):
                        activate(2 * GROUP_UNITS * i + k, k, c)
                    if k < 2 * GROUP_UNITS:
                        for g, wu, w in prepared(i, k, last):
                            round_w(g, wu, w)

            run_groups(act, pair)

        @block.vector
        def _(dve):
            def products(n, k, parity):
                g = n * STEP_HEADS + k
                if k == 0:
                    dve.wait_ge(q_evac, (n + 1) * STEP_BLOCKS)
                if not isinstance(n, int) or g > 1:
                    dve.wait_ge(reduced, g - 1)
                dve.wait_ge(y_evac, (g + 1) * LB)
                y = ysb[k % 2][:, :].rearrange("p (a w) -> p a w", w=YW)
                q = head_view(qT[parity], k, QW)
                p = prod[k % 2][:, :].rearrange("p (a t i) -> p a t i", t=TERMS, i=HD)
                sq = STEP_HEADS * QW
                nc.vector.tensor_tensor(p[:, :, 0:DIAG, :], _pattern(y, [(YW, JB), (QW, DIAG), (1, HD)]),
                                        _pattern(q, [(sq, JB), (1, DIAG), (1, HD)]),
                                        ALU.mult).then_inc(multiplied, 1)
                nc.vector.tensor_tensor(p[:, :, DIAG, :].rearrange("p a (c i) -> p a c i", c=2),
                                        _pattern(y, [(YW, JB), (0, 2), (1, DIAG)], DIAG * QW),
                                        _pattern(q, [(sq, JB), (DIAG, 2), (1, DIAG)], DIAG),
                                        ALU.mult).then_inc(multiplied, 1)

            def reduce(n, k):
                g = n * STEP_HEADS + k
                dve.wait_ge(multiplied, 2 * (g + 1))
                dve.wait_ge(mirrored, g + 1)
                p = prod[k % 2][:, :].rearrange("p (a t i) -> p a i t", t=TERMS, i=HD)
                o = oT[:, :].rearrange("p (a h i) -> p a h i", h=STEP_HEADS, i=HD)[:, :, k % STEP_HEADS, :]
                nc.vector.tensor_reduce(o, p, AX_X, ALU.add).then_inc(reduced, 1)

            def statistics(at, source):
                nc.vector.bn_stats(stats[:, at, :], source).then_inc(stats_done, 1)

            def normalise(at, dst, source, done):
                nc.vector.tensor_scalar(dst, source, meanvar[:, at, 0:1], rstd[:, at:at + 1], ALU.subtract,
                                        ALU.mult).then_inc(done, 1)

            def normalise_query(n, bb):
                normalise(2 + bb, _pattern(qn[:, bb, :], [(P, LB), (-1, P)], P - 1),
                          acc_of(n, bb).rearrange("p (j x) -> p j x", j=LB), q_normed)

            def aggregate(lo, hi, taken):
                wait_apart(dve, stats_done, taken)
                for at in range(lo, hi):
                    ins = nc.vector.bn_aggr(meanvar[:, at, :], stats[:, at, :])
                ins.then_inc(aggr_done, 1)

            dve.wait_ge(kp_loaded, 32)
            dve.wait_ge(consts_ready, 2)
            nc.vector.tensor_copy(_pattern(kp, [(-1, L)], L - 1), k_loaded).then_inc(kp_ready, 1)
            dve.wait_ge(kp_ready, 1)
            nc.vector.tensor_tensor(kp[:, L - 1:L], kp[:, L - 1:L], dcol, ALU.add).then_inc(kp_ready, 1)

            def split_w(g, u, w):
                dve.wait_ge(w_hi, g * W_UNITS + u + 1)
                hi, lo = (part[:, u * 512:(u + 1) * 512] for part in w_slot[(w // W_UNITS) % 2])
                nc.vector.tensor_tensor(lo, ps[:, w_bank(w), :], hi.bitcast(F32),
                                        ALU.subtract).then_inc(w_split, 1)

            for bb in range(STEP_BLOCKS):
                dve.wait_ge(cx_loaded[bb], 16)
                statistics(2 + bb, acc_of(0, bb))
            aggregate(2, 4, STEP_BLOCKS)
            dve.wait_ge(rstd_ready, 1)
            for bb in range(STEP_BLOCKS):
                normalise_query(0, bb)

            def step(n, parity, i):
                conv, prep, post = kinds(n)
                if conv:
                    products(n, 0, parity)
                for u in first_weights(n, 0):
                    split_w(0, u, u)
                if post and conv:
                    reduce(n - 1, 3)
                if conv:
                    products(n, 1, parity)
                for u in first_weights(n, 1):
                    split_w(0, u, u)
                if post:
                    for bb in range(STEP_BLOCKS):
                        dve.wait_ge(o_transposed, (n - 1) * STEP_BLOCKS + bb + 1)
                        nc.vector.tensor_tensor(acc_of(n - 1, bb), ps[:, 4 + bb, :], acc_of(n - 1, bb),
                                                ALU.add).then_inc(o_added, 1)
                if prep:
                    for bb in range(STEP_BLOCKS):
                        wait_apart(dve, cx_loaded[bb], (n + 1) * 32 + 16)
                        statistics(2 + bb, acc_of(n + 1, bb))
                if post:
                    wait_apart(dve, o_added, n * STEP_BLOCKS)
                    for bb in range(STEP_BLOCKS):
                        statistics(bb, acc_of(n - 1, bb))
                done = (n + 2) * STEP_BLOCKS + n * STEP_BLOCKS if prep else (STEPS + n) * STEP_BLOCKS
                aggregate(0 if post else 2, 4 if prep else 2, done)
                if conv:
                    reduce(n, 0)
                    products(n, 2, parity)
                if not conv:
                    multiply(0, 0)
                dve.wait_ge(rstd_ready, n + 2)
                if prep:
                    for bb in range(STEP_BLOCKS):
                        dve.wait_ge(q_transposed, n * STEP_BLOCKS + bb + 1)
                        normalise_query(n + 1, bb)
                if post:
                    for bb in range(STEP_BLOCKS):
                        normalise(bb, hn[:, bb, :], acc_of(n - 1, bb), h_normed)
                if conv:
                    reduce(n, 1)
                    products(n, 3, parity)
                    reduce(n, 2)
                if conv and not prep:
                    reduce(n, 3)
                if not conv:
                    split_a(0, 0, 0)
                if post:
                    for bb in range(STEP_BLOCKS):
                        dve.wait_ge(h_hi, (n - 1) * STEP_BLOCKS + bb + 1)
                        nc.vector.tensor_tensor(hT_of(1, i, 1 - parity, bb), bank3(6 + bb, P),
                                                hT_of(0, i, 1 - parity, bb).bitcast(F32),
                                                ALU.subtract).then_inc(h_split, 1)

            def multiply(u, c):
                dve.wait_ge(silu_ready, CHUNKS * u + c + 1)
                nc.vector.tensor_tensor(a_full[:, c, :], ps[:, 2 * c + 1, :], a_full[:, c, :],
                                        ALU.mult).then_inc(product_done, 1)

            def split_a(u, k, c):
                dve.wait_ge(a_hi, CHUNKS * u + c + 1)
                hi, lo = (part[:, c * TILE:(c + 1) * TILE] for part in a_part[k % 2])
                nc.vector.tensor_tensor(lo, a_full[:, c, :], hi.bitcast(F32), ALU.subtract).then_inc(a_split, 1)

            def add_down(u, k, first, end):
                for q in range(first, end):
                    dve.wait_ge(d_ready, DOWN_FREE + TILE_BLOCKS * u + q + 1)
                    at = (k % GROUP_UNITS * TILE_BLOCKS + q) * L
                    nc.vector.tensor_tensor(acc[:, at:at + L], ps[:, 4 + q % 2, :], acc[:, at:at + L],
                                            ALU.add).then_inc(added, 1)

            run_steps(dve, step)
            multiply(0, 1)
            split_a(0, 0, 1)

            def pair(i, last):
                for k in range(1, 2 * GROUP_UNITS + (not last)):
                    u = 2 * GROUP_UNITS * i + k
                    multiply(u, 0)
                    split_a(u, k, 0)
                    multiply(u, 1)
                    add_down(u - 1, k - 1, 0, 1)
                    split_a(u, k, 1)
                    add_down(u - 1, k - 1, 1, 2)
                    if k < 2 * GROUP_UNITS:
                        for g, wu, w in prepared(i, k, last):
                            split_w(g, wu, w)
                    add_down(u - 1, k - 1, 2, TILE_BLOCKS)
                if last:
                    add_down(u, k, 0, TILE_BLOCKS)

            run_groups(dve, pair)

        @block.tensor
        def _(pe):
            def transposes(b, source, done, permutation=ident):
                for j in range(4):
                    ins = nc.tensor.transpose(ps[:, b, j * P:(j + 1) * P], source(j), permutation[:, :])
                ins.then_inc(done, 1)

            def transpose_c(n):
                for bb in range(STEP_BLOCKS):
                    if isinstance(n, int) and n == 0:
                        pe.wait_ge(first_c_loaded[bb], 16)
                    else:
                        pe.wait_ge(cx_loaded[bb], n * 32 + 16)
                    if not isinstance(n, int) or n > 0:
                        pe.wait_ge(c_evac, (n - 1) * STEP_BLOCKS + bb + 1)
                        pe.wait_ge(h_split, H_FREE + (n - 3) * STEP_BLOCKS + bb + 1 if not isinstance(n, int) or n > 1
                                   else H_FREE)
                    transposes(6 + bb, lambda j: cnat[:, bb, j * P:(j + 1) * P], c_transposed)

            def transpose_q(n):
                for bb in range(STEP_BLOCKS):
                    pe.wait_ge(q_normed, n * STEP_BLOCKS + bb + 1)
                    if not isinstance(n, int) or n > 0:
                        pe.wait_ge(q_evac, (n - 1) * STEP_BLOCKS + bb + 1)
                    if not isinstance(n, int) or n > 1:
                        pe.wait_ge(o_added, (n - 2) * STEP_BLOCKS + bb + 1)
                    transposes(4 + bb, lambda j: qn[:, bb, j * P:(j + 1) * P], q_transposed)

            def transpose_w(g, u, w):
                if w < W_UNITS:
                    source = wnat_first[w]
                    pe.wait_ge(first_loaded[w], 16)
                else:
                    use, slot = divmod(w - W_UNITS, WNAT)
                    source = wnat_later[:, slot, :]
                    pe.wait_ge(wnat_loaded[slot], (g - w // W_UNITS) * (16 * W_UNITS // WNAT) + 16 * (use + 1))
                if w < 2:
                    pe.wait_ge(c_evac, w + 1)
                elif w < 4:
                    pe.wait_ge(q_evac, w - 1)
                else:
                    pe.wait_ge(w_split, g * W_UNITS + u - 1)
                transposes(w_bank(w), lambda j: source[:, j * P:(j + 1) * P], w_transposed)

            def convolve(n, k, parity):
                g = n * STEP_HEADS + k
                pe.wait_ge(toep_loaded[k % 2], (g - k % 2) * 8 + 16)
                pe.wait_ge(kv_ready, g + 1)
                for j in range(LB):
                    if not isinstance(n, int) or g > 0:
                        pe.wait_ge(y_evac, (g - 1) * LB + j + 1)
                    for d in range(j + 1):
                        src = kv[k % 2][:, (j - d) * B * PAIRS:(j - d + 1) * B * PAIRS]
                        ins = nc.tensor.matmul(ps[:, j, 0:B * PAIRS], toep[k % 2][:, (LB - 1 - d) * P:(LB - d) * P], src,
                                               start=d == 0, stop=d == j)
                    ins.then_inc(y_ready, 1)

            pe.wait_ge(ident_ready, 4)
            transpose_c(0)

            def step(n, parity, i):
                conv, prep, post = kinds(n)
                if conv:
                    convolve(n, 0, parity)
                    if isinstance(n, int) and n == 0:
                        transpose_q(0)
                    for u in first_weights(n, 0):
                        transpose_w(0, u, u)
                    convolve(n, 1, parity)
                    for u in first_weights(n, 1):
                        transpose_w(0, u, u)
                else:
                    pe.wait_ge(y_evac, H * LB)
                    pe.wait_ge(h_split, H_FREE + TILE_BLOCKS)
                    gate_up(0, 0, 0)
                if post:
                    pe.wait_ge(reduced, n * STEP_HEADS)
                    for bb in range(STEP_BLOCKS):
                        if prep or conv:
                            pe.wait_ge(q_evac, n * STEP_BLOCKS + bb + 1)
                        else:
                            pe.wait_ge(o_added, (n - 2) * STEP_BLOCKS + bb + 1)
                        transposes(4 + bb, lambda j: oT[:, (j * B + bb * BLOCK_BATCHES) * STEP_ROWS:
                                                                    (j * B + bb * BLOCK_BATCHES) * STEP_ROWS + P],
                                   o_transposed, flip)
                if isinstance(n, int) and n == 0:
                    pe.wait_ge(w_split, 2)
                if prep:
                    transpose_c(n + 1)
                if conv:
                    convolve(n, 2, parity)
                    convolve(n, 3, parity)
                if isinstance(n, int) and n == 0:
                    pe.wait_ge(w_split, W_UNITS)
                if prep:
                    transpose_q(n + 1)
                if not conv:
                    gate_up(0, 0, 1)
                if post:
                    for bb in range(STEP_BLOCKS):
                        pe.wait_ge(h_normed, (n - 1) * STEP_BLOCKS + bb + 1)
                        if prep:
                            pe.wait_ge(c_evac, (n + 1) * STEP_BLOCKS + bb + 1)
                        else:
                            pe.wait_ge(h_split, H_FREE + (n - 2) * STEP_BLOCKS + bb + 1)
                        transposes(6 + bb, lambda j: hn[:, bb, j * P:(j + 1) * P], h_transposed)

            def gate_up(u, k, c):
                slot, t = divmod(k % (2 * GROUP_UNITS), GROUP_UNITS)
                pe.wait_ge(product_done, CHUNKS * u + c + 1)
                for up in range(2):
                    for j in range(LB):
                        for n, (a, b) in enumerate(PARTS):
                            at = (2 * c + up) * 512 + j * P
                            ins = nc.tensor.matmul(
                                ps[:, 2 * c + up, :], w_slot[slot][a][:, at:at + P],
                                hT[b][:, (t * LB + j) * TILE:(t * LB + j + 1) * TILE],
                                start=j == 0 and n == 0, stop=j == LB - 1 and n == 2)
                ins.then_inc(gate_up_ready, 1)

            def down(u, k):
                slot = k // GROUP_UNITS
                pe.wait_ge(a_split, CHUNKS * (u + 1) + A_FREE)
                for q in range(TILE_BLOCKS):
                    pe.wait_ge(added, TILE_BLOCKS * u + q + 1)
                    for c in range(CHUNKS):
                        for n, (a, b) in enumerate(PARTS):
                            ins = nc.tensor.matmul(
                                ps[:, 4 + q % 2, :], a_part[k % 2][a][:, c * TILE + q * P:c * TILE + (q + 1) * P],
                                w_slot[slot][b][:, (2 * CHUNKS + c) * 512:(2 * CHUNKS + c + 1) * 512],
                                start=c == 0 and n == 0, stop=c == CHUNKS - 1 and n == 2)
                    ins.then_inc(d_ready, 1)

            run_steps(pe, step)

            def pair(i, last):
                for k in range(1, 2 * GROUP_UNITS + (not last)):
                    u = 2 * GROUP_UNITS * i + k
                    if k % GROUP_UNITS == 0:
                        pe.wait_ge(w_split, (2 * i + k // GROUP_UNITS + 1) * W_UNITS)
                    gate_up(u, k, 0)
                    gate_up(u, k, 1)
                    if k == 1:
                        pe.wait_ge(h_split, H_FREE + BLOCKS)
                    if k < 2 * GROUP_UNITS:
                        for g, wu, w in prepared(i, k, last):
                            transpose_w(g, wu, w)
                    down(u - 1, k - 1)
                if last:
                    down(u, k)

            run_groups(pe, pair)


def _pattern(ap, pattern, offset=0):
    return bass.AP(tensor=ap.tensor, offset=ap.offset + offset, ap=[list(ap.ap[0])] + [list(q) for q in pattern])


_INS = ["x", "ctx_2048", "L0_xattn_ssm_kernel", "L0_xattn_D", "L0_ffn_w_gate_up", "L0_ffn_w_down"]


def kernel(**inputs):
    import numpy as _np
    import concourse.bacc as _bacc
    from concourse import mybir as _mybir
    from concourse.bass_utils import run_bass_kernel_spmd as _run

    nc = _bacc.Bacc("TRN2", target_bir_lowering=False, num_devices=1)
    arrays, args = {}, []
    for name in _INS:
        a = _np.ascontiguousarray(inputs[name])
        arrays[f"in_{name}"] = a
        args.append(nc.dram_tensor(f"in_{name}", a.shape, _mybir.dt.from_np(a.dtype), kind="ExternalInput").ap())
    shape = inputs["x"].shape
    result = nc.dram_tensor("out_0", shape, _mybir.dt.float32, kind="ExternalOutput").ap()
    xattn_ffn(nc, *args, result)
    r = _run(nc, [arrays], core_ids=[0])
    return r.results[0]["out_0"]
```
